# Optimizing a Trainium2 kernel written in Bass

```python
import numpy as np
import jax
import jax.numpy as jnp

def _softmax(x, axis=-1):
    return jax.nn.softmax(x, axis=axis)
def _gelu(x):
    return jax.nn.gelu(x, approximate=True)
def _silu(x):
    return jax.nn.silu(x)
def _sigmoid(x):
    return jax.nn.sigmoid(x)
def _layernorm(x, axis=-1, eps=1e-5):
    m = jnp.mean(x, axis=axis, keepdims=True)
    v = jnp.var(x, axis=axis, keepdims=True)
    return (x - m) / jnp.sqrt(v + eps)
def _scatter_add(tgt, idx, src, axis=0):
    return tgt.at[idx].add(src)
def _segment_sum(src, seg, n):
    return jax.ops.segment_sum(src, seg, n)

kernel_name = 'mk_conv_seq_d1_conv_nchw512_9b61ac'

def setup_inputs(seed: int = 0):
    np.random.seed(seed)
    _w = jnp.asarray
    def _rec_inputs():
        import jax
        import jax.numpy as jnp
        _gk = jax.random.key(seed)
        x = -7.109e-05 + 0.9999 * jax.random.normal(jax.random.fold_in(_gk, 1), (32, 512, 64, 64), jnp.float32)
        return x
    x = _rec_inputs()
    def _L0_conv_setup():
        import jax, jax.numpy as jnp
        import numpy as np

        def _conv1d(x, w, b):
            pad = (w.shape[-1] - 1) // 2
            y = jax.lax.conv_general_dilated(x, w, window_strides=(1,), padding=[(pad, pad)], dimension_numbers=('NCH', 'OIH', 'NCH'))
            return y + b[None, :, None]
        key = jax.random.key(seed)
        k1, k2, k3, k4, k5 = jax.random.split(key, 5)
        N, C, H, W = (32, 512, 64, 64)
        K = 5
        return {'x': jax.random.normal(k1, (N, C, H, W), dtype=jnp.float32), 'w_q': jax.random.normal(k2, (1, 1, K), dtype=jnp.float32) * 0.3, 'b_q': jax.random.normal(k3, (1,), dtype=jnp.float32) * 0.1, 'w_loc': jax.random.normal(k4, (1, 1, K), dtype=jnp.float32) * 0.3, 'b_loc': jax.random.normal(k5, (1,), dtype=jnp.float32) * 0.1}
    _L0_conv_all = _L0_conv_setup()
    _L0_conv_in = {k: v for k, v in _L0_conv_all.items() if k in ('w_q', 'b_q', 'w_loc', 'b_loc', )}
    del _L0_conv_all

    return {
        "x": x,
        "L0_conv_w_q": _L0_conv_in["w_q"],
        "L0_conv_b_q": _L0_conv_in["b_q"],
        "L0_conv_w_loc": _L0_conv_in["w_loc"],
        "L0_conv_b_loc": _L0_conv_in["b_loc"],
    }

def reference(x, L0_conv_w_q, L0_conv_b_q, L0_conv_w_loc, L0_conv_b_loc):
    import jax
    import jax.numpy as jnp
    def _L0_conv_ref(x, w_q, b_q, w_loc, b_loc):
        import jax, jax.numpy as jnp
        import numpy as np

        def _conv1d(x, w, b):
            pad = (w.shape[-1] - 1) // 2
            y = jax.lax.conv_general_dilated(x, w, window_strides=(1,), padding=[(pad, pad)], dimension_numbers=('NCH', 'OIH', 'NCH'))
            return y + b[None, :, None]
        N, C, H, W = x.shape
        xl, xr = jnp.split(x, 2, axis=1)
        Ch = C // 2
        g = jnp.mean(xl, axis=(2, 3)).reshape(N, 1, Ch)
        q = jax.nn.sigmoid(_conv1d(g, w_q, b_q))[:, 0, :]
        qk = q[:, :, None] * q[:, None, :]
        qk = jax.nn.softmax(qk.reshape(N, Ch * Ch), axis=-1).reshape(N, Ch, Ch)
        value = xl.transpose(0, 2, 3, 1).reshape(N, H * W, Ch)
        att = jnp.einsum('npc,ncd->ndp', value, qk).reshape(N, Ch, H, W)
        x1 = xl * att
        gl = jnp.mean(xr, axis=(2, 3)).reshape(N, 1, Ch)
        al = jax.nn.sigmoid(_conv1d(gl, w_loc, b_loc)).reshape(N, Ch, 1, 1)
        x2 = xr * al + xr
        return jnp.concatenate([x1, x2], axis=1) + x

    def _gn(v, G=32, eps=1e-5):
        B_, C_, H_, W_ = v.shape
        g = v.reshape(B_, G, C_ // G, H_, W_)
        m = jnp.mean(g, axis=(2, 3, 4), keepdims=True)
        s = jnp.var(g, axis=(2, 3, 4), keepdims=True)
        return ((g - m) / jnp.sqrt(s + eps)).reshape(v.shape)

    def _ln_c(v, eps=1e-6):
        m = jnp.mean(v, axis=1, keepdims=True)
        s = jnp.var(v, axis=1, keepdims=True)
        return (v - m) / jnp.sqrt(s + eps)

    def _ln_t(v, eps=1e-5):
        m = jnp.mean(v, axis=-1, keepdims=True)
        s = jnp.var(v, axis=-1, keepdims=True)
        return (v - m) / jnp.sqrt(s + eps)

    def _to_tokens(v):
        B_, C_, H_, W_ = v.shape
        return v.reshape(B_, C_, H_ * W_).transpose(0, 2, 1)
    def _from_tokens(t, like):
        B_, C_, H_, W_ = like.shape
        return t.transpose(0, 2, 1).reshape(B_, C_, H_, W_)

    x = _L0_conv_ref(x, L0_conv_w_q, L0_conv_b_q, L0_conv_w_loc, L0_conv_b_loc)
    return x


_drawn_inputs = setup_inputs


def setup_inputs(seed=0):
    import zlib

    import numpy as np

    out = dict(_drawn_inputs(seed))
    spreads = {}
    factors = {'L0_conv_w_q': 64.0, 'L0_conv_w_loc': 32.134}
    for name, (base, spread) in spreads.items():
        noise = np.random.default_rng([zlib.crc32(name.encode()), seed]).standard_normal(out[name].shape)
        drawn = base * np.exp(spread * noise) if base else spread * noise
        out[name] = jnp.asarray(drawn.astype(out[name].dtype))
    for name, factor in factors.items():
        out[name] = (out[name] * factor).astype(out[name].dtype)
    return out
```

```python
import concourse.bass as bass
from concourse import mybir
from contextlib import ExitStack


def gated_channel_kernel(nc: bass.Bass, x: bass.AP, w_q: bass.AP, b_q: bass.AP,
                         w_loc: bass.AP, b_loc: bass.AP, out: bass.AP):
    fp32 = mybir.dt.float32
    bf16 = mybir.dt.bfloat16
    ALU = mybir.AluOpType
    ACT = mybir.ActivationFunctionType
    AX = mybir.AxisListType

    N, C, H, W = x.shape
    P = 128
    HW = H * W
    CH = C // 2
    T = CH // P
    K = w_q.shape[2]
    PAD = (K - 1) // 2
    SLOTS = 3
    SUM = HW // 2
    NS = HW // SUM
    GC = 512
    G = HW // GC
    GBUF = 3
    SG = G // 2
    HEAD = SLOTS
    TURNS = (N - HEAD) // SLOTS
    TAIL = N - HEAD - TURNS * SLOTS

    x_t = x.rearrange("n (t p) h w -> n t p (h w)", p=P)
    out_t = out.rearrange("n (t p) h w -> n t p (h w)", p=P)
    out_p = out.rearrange("n (t p) h w -> n p t (h w)", p=P)

    ctx = ExitStack()
    with ctx:
        def sb(name, shape, dt=fp32):
            return ctx.enter_context(nc.sbuf_tensor(name, shape, dt))

        def pb(name, shape):
            return ctx.enter_context(nc.psum_tensor(name, shape, fp32))

        def sem(name):
            return ctx.enter_context(nc.semaphore(name))

        img = sb("img", [P, SLOTS, 2 * T, HW])
        band_q = sb("band_q", [P, T, CH])
        band_loc = sb("band_loc", [P, T, CH])
        sum_junk = sb("sum_junk", [P, SUM], bf16)
        left_sum = sb("left_sum", [P, T, NS])
        right_sum = sb("right_sum", [P, T, NS])
        left_rep = sb("left_rep", [P, T, P])
        right_tot = sb("right_tot", [P, T])
        q_buf = sb("q_buf", [P, CH + T])
        q_max = sb("q_max", [P, 1])
        neg_max = sb("neg_max", [P, 1])
        exp_qq = sb("exp_qq", [P, T, CH])
        row_sum = sb("row_sum", [P, T])
        inv_total = sb("inv_total", [P, 1])
        prob = sb("prob", [P, T, CH])
        al_buf = sb("al_buf", [P, T])
        ones = sb("ones", [P, P])
        taps_q = sb("taps_q", [P, K])
        taps_loc = sb("taps_loc", [P, K])
        bias = sb("bias", [P, 2])
        neg_bias = sb("neg_bias", [P, 2])
        diag = img[:, SLOTS - 1, 0, 0:K * T * CH // 2].bitcast(bf16).rearrange(
            "p (k t d) -> p k t d", k=K, t=T)

        att = pb("att", [P, GBUF, T, GC])
        z_left = pb("z_left", [P, GC])
        z_right = pb("z_right", [P, GC])
        TOTAL = CH + T

        const_loaded = sem("const_loaded")
        loaded = [[sem(f"loaded_s{s}_t{t}") for t in range(2 * T)] for s in range(SLOTS)]
        left_stored = [[sem(f"left_stored_s{s}_{h}") for h in range(G // SG)] for s in range(SLOTS)]
        right_stored = [[sem(f"right_stored_s{s}_{t}") for t in range(T)] for s in range(SLOTS)]
        diag_zeroed = sem("diag_zeroed")
        diag_ready = sem("diag_ready")
        ones_ready = sem("ones_ready")
        band_zeroed = sem("band_zeroed")
        band_step = sem("band_step")
        neg_bias_ready = sem("neg_bias_ready")
        left_summed = sem("left_summed")
        left_rep_ready = sem("left_rep_ready")
        z_left_ready = sem("z_left_ready")
        q_exp_ready = sem("q_exp_ready")
        q_den_ready = sem("q_den_ready")
        q_ready = sem("q_ready")
        q_max_ready = sem("q_max_ready")
        neg_max_ready = sem("neg_max_ready")
        exp_qq_ready = sem("exp_qq_ready")
        total_ready = sem("total_ready")
        inv_total_ready = sem("inv_total_ready")
        prob_ready = sem("prob_ready")
        att_ready = sem("att_ready")
        left_done = sem("left_done")
        right_summed = sem("right_summed")
        right_tot_ready = sem("right_tot_ready")
        z_right_ready = sem("z_right_ready")
        al_exp_ready = sem("al_exp_ready")
        al_den_ready = sem("al_den_ready")
        al_ready = sem("al_ready")
        gain_ready = sem("gain_ready")
        right_done = sem("right_done")

        def images(engine, step):
            for n in range(HEAD):
                step(n, n // SLOTS, n % SLOTS, n)
            with engine.Fori(0, TURNS) as turn:
                for j in range(SLOTS):
                    step(turn * SLOTS + (HEAD + j), turn + 1, j, None)
            for n in range(N - TAIL, N):
                step(n, n // SLOTS, n % SLOTS, n)

        block = ctx.enter_context(nc.Block())

        @block.sync
        def _(sp):
            sp.dma_start(img[:, 0, 0, :], x_t[0, 0]).then_inc(loaded[0][0], 16)
            sp.dma_start(taps_q[:, :], w_q[0, 0:1, :].partition_broadcast(P)).then_inc(const_loaded, 16)
            sp.dma_start(taps_loc[:, :], w_loc[0, 0:1, :].partition_broadcast(P)).then_inc(const_loaded, 16)
            sp.dma_start(bias[:, 0:1], b_q.rearrange("(a b) -> a b", a=1).partition_broadcast(P))\
                .then_inc(const_loaded, 16)
            sp.dma_start(bias[:, 1:2], b_loc.rearrange("(a b) -> a b", a=1).partition_broadcast(P))\
                .then_inc(const_loaded, 16)

            def load(n, use, slot, static):
                first = static is not None and static < SLOTS
                if static == SLOTS - 1:
                    sp.wait_ge(band_step, 2 * K)
                if not first:
                    for h in range(G // SG):
                        sp.wait_ge(left_stored[slot][h], 16 * use)
                for t in range(2 * T):
                    if not first and t >= T:
                        sp.wait_ge(right_stored[slot][t - T], 16 * use)
                    if static == 0 and t == 0:
                        continue
                    sp.dma_start(img[:, slot, t, :], x_t[n, t]).then_inc(loaded[slot][t], 16)

            images(sp, load)

        @block.gpsimd
        def _(pool):
            nc.gpsimd.memset(img[:, SLOTS - 1, 0, 0:K * T * CH // 2], 0.0).then_inc(diag_zeroed, 1)
            nc.gpsimd.memset(ones[:, :], 1.0).then_inc(ones_ready, 1)
            pool.wait_ge(diag_zeroed, 1)
            for k in range(K):
                nc.gpsimd.affine_select(out=diag[:, k], in_=diag[:, k], compare_op=ALU.not_equal, fill=1.0,
                                        base=PAD - k, pattern=[[P, T], [-1, CH]], channel_multiplier=1)\
                    .then_inc(diag_ready, 1)

            def store(n, use, slot, static):
                for h in range(G // SG):
                    pool.wait_ge(left_done, n * G + (h + 1) * SG)
                    lo = h * SG * GC
                    pool.dma_start(out_p[n, :, 0:T, lo:lo + SG * GC], img[:, slot, 0:T, lo:lo + SG * GC])\
                        .then_inc(left_stored[slot][h], 16)
                    if h == 0:
                        for t in range(T):
                            pool.wait_ge(right_done, n * T + t + 1)
                            pool.dma_start(out_t[n, T + t], img[:, slot, T + t, :])\
                                .then_inc(right_stored[slot][t], 16)

            images(pool, store)
            for s in range(SLOTS):
                uses = (N - s + SLOTS - 1) // SLOTS
                for done in left_stored[s] + right_stored[s]:
                    pool.wait_ge(done, 16 * uses)

        @block.scalar
        def _(act):
            act.wait_ge(neg_bias_ready, 1)

            def sums(n, use, slot, first_tile, into, done):
                for t in range(T):
                    act.wait_ge(loaded[slot][first_tile + t], 16 * (use + 1))
                    for s in range(NS):
                        if t or s:
                            act.wait_ge(done, n * T * NS + t * NS + s)
                        nc.scalar.activation(sum_junk[:, :], img[:, slot, first_tile + t, s * SUM:(s + 1) * SUM],
                                             ACT.Copy, accum_out=into[:, t, s:s + 1]).then_inc(done, 1)

            def step(n, use, slot, static):
                sums(n, use, slot, 0, left_sum, left_summed)
                act.wait_ge(z_left_ready, n + 1)
                nc.scalar.activation(q_buf[:, :], z_left[:, 0:CH + T], ACT.Exp, bias=neg_bias[:, 0:1],
                                     scale=-1.0 / HW).then_inc(q_exp_ready, 1)
                act.wait_ge(neg_max_ready, n + 1)
                for t in range(T):
                    nc.scalar.activation(exp_qq[:, t, :], q_buf[:, 0:CH], ACT.Exp, bias=neg_max[:, 0:1],
                                         scale=q_buf[:, CH + t:CH + t + 1], accum_out=row_sum[:, t:t + 1])\
                        .then_inc(exp_qq_ready, 1)
                sums(n, use, slot, T, right_sum, right_summed)
                act.wait_ge(z_right_ready, n + 1)
                nc.scalar.activation(al_buf[:, :], z_right[:, 0:T], ACT.Exp, bias=neg_bias[:, 1:2],
                                     scale=-1.0 / HW).then_inc(al_exp_ready, 1)

            images(act, step)

        @block.vector
        def _(dve):
            nc.vector.memset(band_q[:, :, :], 0.0).then_inc(band_zeroed, 1)
            nc.vector.memset(band_loc[:, :, :], 0.0).then_inc(band_zeroed, 1)
            dve.wait_ge(const_loaded, 16 * 4)
            nc.vector.tensor_scalar(neg_bias[:, :], bias[:, :], -1.0, None, ALU.mult).then_inc(neg_bias_ready, 1)
            dve.wait_ge(band_zeroed, 2)
            for k in range(K):
                dve.wait_ge(diag_ready, k + 1)
                for i, (band, taps) in enumerate(((band_q, taps_q), (band_loc, taps_loc))):
                    if k > 0:
                        dve.wait_ge(band_step, 2 * (k - 1) + i + 1)
                    nc.vector.scalar_tensor_tensor(band[:, :, :], diag[:, k], taps[:, k:k + 1], band[:, :, :],
                                                   ALU.mult, ALU.add).then_inc(band_step, 1)
            dve.wait_ge(ones_ready, 1)

            def products(n, slot, lo, hi):
                for g in range(lo, hi):
                    dve.wait_ge(att_ready, n * G + g + 1)
                    xl = img[:, slot, 0:T, g * GC:(g + 1) * GC]
                    buf = (slot * G + g) % GBUF
                    nc.vector.scalar_tensor_tensor(xl, att[:, buf], 1.0, xl, ALU.add, ALU.mult)\
                        .then_inc(left_done, 1)

            def step(n, use, slot, static):
                dve.wait_ge(left_summed, (n + 1) * T * NS)
                for t in range(T):
                    nc.vector.tensor_scalar(left_rep[:, t, :], ones[:, :], left_sum[:, t, 0:1],
                                            left_sum[:, t, 1:2], ALU.mult, ALU.add).then_inc(left_rep_ready, 1)
                dve.wait_ge(q_exp_ready, n + 1)
                nc.vector.tensor_scalar(q_buf[:, :], q_buf[:, :], 1.0, None, ALU.add).then_inc(q_den_ready, 1)
                dve.wait_ge(q_den_ready, n + 1)
                nc.vector.reciprocal(q_buf[:, :], q_buf[:, :]).then_inc(q_ready, 1)
                dve.wait_ge(q_ready, n + 1)
                nc.vector.tensor_reduce(q_max[:, :], q_buf[:, 0:CH], AX.X, ALU.max).then_inc(q_max_ready, 1)
                dve.wait_ge(q_max_ready, n + 1)
                nc.vector.tensor_scalar(neg_max[:, :], q_max[:, :], q_max[:, 0:1], -1.0, ALU.mult, ALU.mult)\
                    .then_inc(neg_max_ready, 1)
                dve.wait_ge(total_ready, n + 1)
                nc.vector.reciprocal(inv_total[:, :], z_left[:, TOTAL:TOTAL + 1]).then_inc(inv_total_ready, 1)
                dve.wait_ge(inv_total_ready, n + 1)
                if static != 0:
                    dve.wait_ge(att_ready, n * G)
                nc.vector.tensor_scalar(prob[:, :, :], exp_qq[:, :, :], inv_total[:, 0:1], None, ALU.mult)\
                    .then_inc(prob_ready, 1)
                products(n, slot, 0, SG)
                dve.wait_ge(right_summed, (n + 1) * T * NS)
                nc.vector.tensor_tensor(right_tot[:, :], right_sum[:, :, 0], right_sum[:, :, 1], ALU.add)\
                    .then_inc(right_tot_ready, 1)
                dve.wait_ge(al_exp_ready, n + 1)
                nc.vector.tensor_scalar(al_buf[:, :], al_buf[:, :], 1.0, None, ALU.add).then_inc(al_den_ready, 1)
                dve.wait_ge(al_den_ready, n + 1)
                nc.vector.reciprocal(al_buf[:, :], al_buf[:, :]).then_inc(al_ready, 1)
                dve.wait_ge(al_ready, n + 1)
                nc.vector.tensor_scalar(al_buf[:, :], al_buf[:, :], 2.0, None, ALU.add).then_inc(gain_ready, 1)
                dve.wait_ge(gain_ready, n + 1)
                for t in range(T):
                    xr = img[:, slot, T + t, :]
                    nc.vector.tensor_scalar(xr, xr, al_buf[:, t:t + 1], None, ALU.mult).then_inc(right_done, 1)
                products(n, slot, SG, G)

            images(dve, step)

        @block.tensor
        def _(pe):
            pe.wait_ge(ones_ready, 1)
            pe.wait_ge(band_step, 2 * K)

            def products(n, slot, static, lo, hi):
                for g in range(lo, hi):
                    buf = (slot * G + g) % GBUF
                    if static != 0 or g >= GBUF:
                        pe.wait_ge(left_done, n * G + g - GBUF + 1)
                    for d in range(T):
                        for c in range(T):
                            last = nc.tensor.matmul(att[:, buf, d, :], prob[:, c, d * P:(d + 1) * P],
                                                    img[:, slot, c, g * GC:(g + 1) * GC],
                                                    start=(c == 0), stop=(c == T - 1))
                    last.then_inc(att_ready, 1)

            def step(n, use, slot, static):
                pe.wait_ge(left_rep_ready, (n + 1) * T)
                for c in range(T):
                    nc.tensor.matmul(z_left[:, 0:CH], left_rep[:, c, :], band_q[:, c, :],
                                     start=(c == 0), stop=(c == T - 1))
                for d in range(T):
                    for c in range(T):
                        last = nc.tensor.matmul(z_left[:, CH + d:CH + d + 1], band_q[:, c, d * P:(d + 1) * P],
                                                left_rep[:, c, 0:1], start=(c == 0), stop=(c == T - 1))
                last.then_inc(z_left_ready, 1)
                pe.wait_ge(exp_qq_ready, (n + 1) * T)
                for c in range(T):
                    last = nc.tensor.matmul(z_left[:, TOTAL:TOTAL + 1], ones[:, :], row_sum[:, c:c + 1],
                                            start=(c == 0), stop=(c == T - 1))
                last.then_inc(total_ready, 1)
                pe.wait_ge(prob_ready, n + 1)
                products(n, slot, static, 0, SG)
                pe.wait_ge(right_tot_ready, n + 1)
                for d in range(T):
                    for c in range(T):
                        last = nc.tensor.matmul(z_right[:, d:d + 1], band_loc[:, c, d * P:(d + 1) * P],
                                                right_tot[:, c:c + 1], start=(c == 0), stop=(c == T - 1))
                last.then_inc(z_right_ready, 1)
                products(n, slot, static, SG, G)

            images(pe, step)


_INS = ['x', 'L0_conv_w_q', 'L0_conv_b_q', 'L0_conv_w_loc', 'L0_conv_b_loc']


def kernel(**inputs):
    import numpy as _np
    import concourse.bacc as _bacc
    from concourse import mybir as _mybir
    from concourse.bass_utils import run_bass_kernel_spmd as _run

    nc = _bacc.Bacc("TRN2", target_bir_lowering=False, num_devices=1)
    arrays, args = {}, []
    for name in _INS:
        a = _np.ascontiguousarray(inputs[name])
        arrays[f"in_{name}_dram"] = a
        args.append(nc.dram_tensor(f"in_{name}_dram", a.shape, _mybir.dt.from_np(a.dtype), kind="ExternalInput").ap())
    args.append(nc.dram_tensor("out_0_dram", inputs['x'].shape, _mybir.dt.float32, kind="ExternalOutput").ap())
    gated_channel_kernel(nc, *args)
    r = _run(nc, [arrays], core_ids=[0])
    return r.results[0]["out_0_dram"]
```

```python
import concourse.bass as bass
from concourse import mybir
from contextlib import ExitStack


def gated_channel_kernel(nc: bass.Bass, x: bass.AP, w_q: bass.AP, b_q: bass.AP,
                         w_loc: bass.AP, b_loc: bass.AP, out: bass.AP):
    fp32 = mybir.dt.float32
    bf16 = mybir.dt.bfloat16
    ALU = mybir.AluOpType
    ACT = mybir.ActivationFunctionType
    AX = mybir.AxisListType

    N, C, H, W = x.shape
    P = 128
    HW = H * W
    CH = C // 2
    T = CH // P
    K = w_q.shape[2]
    PAD = (K - 1) // 2
    SLOTS = 3
    SUM = HW // 2
    NS = HW // SUM
    GC = 512
    G = HW // GC
    GBUF = 3
    SG = G // 2
    RIGHT_CONV_AFTER, LEFT_CONV_AFTER, TOTAL_AFTER = 0, 5, 6
    HEAD = SLOTS
    TURNS = (N - HEAD) // SLOTS
    TAIL = N - HEAD - TURNS * SLOTS

    x_t = x.rearrange("n (t p) h w -> n t p (h w)", p=P)
    out_t = out.rearrange("n (t p) h w -> n t p (h w)", p=P)
    out_p = out.rearrange("n (t p) h w -> n p t (h w)", p=P)

    ctx = ExitStack()
    with ctx:
        def sb(name, shape, dt=fp32):
            return ctx.enter_context(nc.sbuf_tensor(name, shape, dt))

        def pb(name, shape):
            return ctx.enter_context(nc.psum_tensor(name, shape, fp32))

        def sem(name):
            return ctx.enter_context(nc.semaphore(name))

        img = sb("img", [P, SLOTS, 2 * T, HW])
        band_q = sb("band_q", [P, T, CH])
        band_loc = sb("band_loc", [P, T, CH])
        sum_junk = sb("sum_junk", [P, SUM], bf16)
        left_sum = sb("left_sum", [P, T, NS])
        right_sum = sb("right_sum", [P, T, NS])
        left_rep = sb("left_rep", [P, T, P])
        right_tot = sb("right_tot", [P, T])
        q_buf = sb("q_buf", [P, CH + T])
        q_max = sb("q_max", [P, 1])
        neg_max = sb("neg_max", [P, 1])
        exp_qq = sb("exp_qq", [P, T, CH])
        row_sum = sb("row_sum", [P, T])
        inv_total = sb("inv_total", [P, 1])
        prob = sb("prob", [P, T, CH])
        al_buf = sb("al_buf", [P, T])
        ones = sb("ones", [P, P])
        taps_q = sb("taps_q", [P, K])
        taps_loc = sb("taps_loc", [P, K])
        bias = sb("bias", [P, 2])
        neg_bias = sb("neg_bias", [P, 2])
        diag = img[:, SLOTS - 1, 0, 0:K * T * CH // 2].bitcast(bf16).rearrange(
            "p (k t d) -> p k t d", k=K, t=T)

        att = pb("att", [P, GBUF, T, GC])
        z_left = pb("z_left", [P, GC])
        z_right = pb("z_right", [P, GC])
        TOTAL = CH + T

        const_loaded = sem("const_loaded")
        loaded = [[sem(f"loaded_s{s}_t{t}") for t in range(2 * T)] for s in range(SLOTS)]
        left_stored = [[sem(f"left_stored_s{s}_{h}") for h in range(G // SG)] for s in range(SLOTS)]
        right_stored = [[sem(f"right_stored_s{s}_{t}") for t in range(T)] for s in range(SLOTS)]
        diag_zeroed = sem("diag_zeroed")
        diag_ready = sem("diag_ready")
        ones_ready = sem("ones_ready")
        band_zeroed = sem("band_zeroed")
        band_step = sem("band_step")
        neg_bias_ready = sem("neg_bias_ready")
        left_summed = sem("left_summed")
        left_rep_ready = sem("left_rep_ready")
        z_left_ready = sem("z_left_ready")
        q_exp_ready = sem("q_exp_ready")
        q_den_ready = sem("q_den_ready")
        q_ready = sem("q_ready")
        q_max_ready = sem("q_max_ready")
        neg_max_ready = sem("neg_max_ready")
        exp_qq_ready = sem("exp_qq_ready")
        total_ready = sem("total_ready")
        inv_total_ready = sem("inv_total_ready")
        prob_ready = sem("prob_ready")
        att_ready = sem("att_ready")
        left_done = sem("left_done")
        right_summed = sem("right_summed")
        right_tot_ready = sem("right_tot_ready")
        z_right_ready = sem("z_right_ready")
        al_exp_ready = sem("al_exp_ready")
        al_den_ready = sem("al_den_ready")
        al_ready = sem("al_ready")
        gain_ready = sem("gain_ready")
        right_done = sem("right_done")

        def images(engine, step):
            for n in range(HEAD):
                step(n, n // SLOTS, n % SLOTS, n)
            with engine.Fori(0, TURNS) as turn:
                for j in range(SLOTS):
                    step(turn * SLOTS + (HEAD + j), turn + 1, j, None)
            for n in range(N - TAIL, N):
                step(n, n // SLOTS, n % SLOTS, n)

        block = ctx.enter_context(nc.Block())

        @block.sync
        def _(sp):
            def load(n, slot, tiles):
                for t in tiles:
                    sp.dma_start(img[:, slot, t, :], x_t[n, t]).then_inc(loaded[slot][t], 16)

            load(0, 0, range(0, 1))
            for dst, src in ((taps_q[:, :], w_q[0, 0:1, :]), (taps_loc[:, :], w_loc[0, 0:1, :]),
                             (bias[:, 0:1], b_q.rearrange("(a b) -> a b", a=1)),
                             (bias[:, 1:2], b_loc.rearrange("(a b) -> a b", a=1))):
                sp.dma_start(dst, src.partition_broadcast(P)).then_inc(const_loaded, 16)
            load(0, 0, range(1, 2 * T))
            for n in range(1, SLOTS):
                if n == SLOTS - 1:
                    sp.wait_ge(band_step, 2 * K)
                load(n, n, range(2 * T))

            def store_left(n, slot, h):
                sp.wait_ge(left_done, n * G + (h + 1) * SG)
                lo = h * SG * GC
                sp.dma_start(out_p[n, :, 0:T, lo:lo + SG * GC], img[:, slot, 0:T, lo:lo + SG * GC])\
                    .then_inc(left_stored[slot][h], 16)

            def step(n, use, slot, static):
                store_left(n, slot, 0)
                for t in range(T):
                    sp.wait_ge(right_done, n * T + t + 1)
                    sp.dma_start(out_t[n, T + t], img[:, slot, T + t, :]).then_inc(right_stored[slot][t], 16)
                if static is None or 0 < static <= N - SLOTS:
                    prev = (slot + SLOTS - 1) % SLOTS
                    prev_uses = use + (slot > 0)
                    for h in range(G // SG):
                        sp.wait_ge(left_stored[prev][h], 16 * prev_uses)
                    load(n + SLOTS - 1, prev, range(T))
                    for t in range(T):
                        sp.wait_ge(right_stored[prev][t], 16 * prev_uses)
                        load(n + SLOTS - 1, prev, range(T + t, T + t + 1))
                store_left(n, slot, 1)

            images(sp, step)
            for s in range(SLOTS):
                uses = (N - s + SLOTS - 1) // SLOTS
                for done in left_stored[s] + right_stored[s]:
                    sp.wait_ge(done, 16 * uses)

        @block.gpsimd
        def _(pool):
            nc.gpsimd.memset(img[:, SLOTS - 1, 0, 0:K * T * CH // 2], 0.0).then_inc(diag_zeroed, 1)
            nc.gpsimd.memset(ones[:, :], 1.0).then_inc(ones_ready, 1)
            pool.wait_ge(diag_zeroed, 1)
            for k in range(K):
                nc.gpsimd.affine_select(out=diag[:, k], in_=diag[:, k], compare_op=ALU.not_equal, fill=1.0,
                                        base=PAD - k, pattern=[[P, T], [-1, CH]], channel_multiplier=1)\
                    .then_inc(diag_ready, 1)

        @block.scalar
        def _(act):
            act.wait_ge(neg_bias_ready, 1)

            def sums(n, use, slot, first_tile, into, done):
                for t in range(T):
                    act.wait_ge(loaded[slot][first_tile + t], 16 * (use + 1))
                    for s in range(NS):
                        if t or s:
                            act.wait_ge(done, n * T * NS + t * NS + s)
                        nc.scalar.activation(sum_junk[:, :], img[:, slot, first_tile + t, s * SUM:(s + 1) * SUM],
                                             ACT.Copy, accum_out=into[:, t, s:s + 1]).then_inc(done, 1)

            def q_exps(n):
                act.wait_ge(z_left_ready, n + 1)
                nc.scalar.activation(q_buf[:, :], z_left[:, 0:CH + T], ACT.Exp, bias=neg_bias[:, 0:1],
                                     scale=-1.0 / HW).then_inc(q_exp_ready, 1)
                act.wait_ge(neg_max_ready, n + 1)
                for t in range(T):
                    nc.scalar.activation(exp_qq[:, t, :], q_buf[:, 0:CH], ACT.Exp, bias=neg_max[:, 0:1],
                                         scale=q_buf[:, CH + t:CH + t + 1], accum_out=row_sum[:, t:t + 1])\
                        .then_inc(exp_qq_ready, 1)

            sums(0, 0, 0, 0, left_sum, left_summed)
            q_exps(0)

            def step(n, use, slot, static):
                sums(n, use, slot, T, right_sum, right_summed)
                act.wait_ge(z_right_ready, n + 1)
                nc.scalar.activation(al_buf[:, :], z_right[:, 0:T], ACT.Exp, bias=neg_bias[:, 1:2],
                                     scale=-1.0 / HW).then_inc(al_exp_ready, 1)
                if static != N - 1:
                    nxt = (slot + 1) % SLOTS
                    sums(n + 1, use + (nxt == 0), nxt, 0, left_sum, left_summed)
                    q_exps(n + 1)

            images(act, step)

        @block.vector
        def _(dve):
            nc.vector.memset(band_q[:, :, :], 0.0).then_inc(band_zeroed, 1)
            nc.vector.memset(band_loc[:, :, :], 0.0).then_inc(band_zeroed, 1)
            dve.wait_ge(const_loaded, 16 * 4)
            nc.vector.tensor_scalar(neg_bias[:, :], bias[:, :], -1.0, None, ALU.mult).then_inc(neg_bias_ready, 1)
            dve.wait_ge(band_zeroed, 2)
            for k in range(K):
                dve.wait_ge(diag_ready, k + 1)
                for i, (band, taps) in enumerate(((band_q, taps_q), (band_loc, taps_loc))):
                    if k > 0:
                        dve.wait_ge(band_step, 2 * (k - 1) + i + 1)
                    nc.vector.scalar_tensor_tensor(band[:, :, :], diag[:, k], taps[:, k:k + 1], band[:, :, :],
                                                   ALU.mult, ALU.add).then_inc(band_step, 1)
            dve.wait_ge(ones_ready, 1)

            def product(n, slot, g):
                dve.wait_ge(att_ready, n * G + g + 1)
                xl = img[:, slot, 0:T, g * GC:(g + 1) * GC]
                nc.vector.scalar_tensor_tensor(xl, att[:, (slot * G + g) % GBUF], 1.0, xl, ALU.add, ALU.mult)\
                    .then_inc(left_done, 1)

            def repeat_sums(n):
                dve.wait_ge(left_summed, (n + 1) * T * NS)
                for t in range(T):
                    nc.vector.tensor_scalar(left_rep[:, t, :], ones[:, :], left_sum[:, t, 0:1],
                                            left_sum[:, t, 1:2], ALU.mult, ALU.add).then_inc(left_rep_ready, 1)

            def queries(n):
                dve.wait_ge(q_exp_ready, n + 1)
                nc.vector.tensor_scalar(q_buf[:, :], q_buf[:, :], 1.0, None, ALU.add).then_inc(q_den_ready, 1)
                dve.wait_ge(q_den_ready, n + 1)
                nc.vector.reciprocal(q_buf[:, :], q_buf[:, :]).then_inc(q_ready, 1)
                dve.wait_ge(q_ready, n + 1)
                nc.vector.tensor_reduce(q_max[:, :], q_buf[:, 0:CH], AX.X, ALU.max).then_inc(q_max_ready, 1)
                dve.wait_ge(q_max_ready, n + 1)
                nc.vector.tensor_scalar(neg_max[:, :], q_max[:, :], q_max[:, 0:1], -1.0, ALU.mult, ALU.mult)\
                    .then_inc(neg_max_ready, 1)

            def probabilities(n, first):
                dve.wait_ge(total_ready, n + 1)
                nc.vector.reciprocal(inv_total[:, :], z_left[:, TOTAL:TOTAL + 1]).then_inc(inv_total_ready, 1)
                dve.wait_ge(inv_total_ready, n + 1)
                if not first:
                    dve.wait_ge(att_ready, n * G)
                nc.vector.tensor_scalar(prob[:, :, :], exp_qq[:, :, :], inv_total[:, 0:1], None, ALU.mult)\
                    .then_inc(prob_ready, 1)

            def right_totals(n):
                dve.wait_ge(right_summed, (n + 1) * T * NS)
                nc.vector.tensor_tensor(right_tot[:, :], right_sum[:, :, 0], right_sum[:, :, 1], ALU.add)\
                    .then_inc(right_tot_ready, 1)

            def right_half(n, slot):
                dve.wait_ge(al_exp_ready, n + 1)
                nc.vector.tensor_scalar(al_buf[:, :], al_buf[:, :], 1.0, None, ALU.add).then_inc(al_den_ready, 1)
                dve.wait_ge(al_den_ready, n + 1)
                nc.vector.reciprocal(al_buf[:, :], al_buf[:, :]).then_inc(al_ready, 1)
                dve.wait_ge(al_ready, n + 1)
                nc.vector.tensor_scalar(al_buf[:, :], al_buf[:, :], 2.0, None, ALU.add).then_inc(gain_ready, 1)
                dve.wait_ge(gain_ready, n + 1)
                for t in range(T):
                    xr = img[:, slot, T + t, :]
                    nc.vector.tensor_scalar(xr, xr, al_buf[:, t:t + 1], None, ALU.mult).then_inc(right_done, 1)

            repeat_sums(0)
            queries(0)
            probabilities(0, True)

            def step(n, use, slot, static):
                for g in range(G):
                    if g == G - 1 and static != N - 1:
                        probabilities(n + 1, False)
                    if g == RIGHT_CONV_AFTER:
                        right_totals(n)
                    product(n, slot, g)
                    if g == RIGHT_CONV_AFTER:
                        right_half(n, slot)
                    if g == LEFT_CONV_AFTER - 1 and static != N - 1:
                        repeat_sums(n + 1)
                    if g == LEFT_CONV_AFTER and static != N - 1:
                        queries(n + 1)

            images(dve, step)

        @block.tensor
        def _(pe):
            pe.wait_ge(ones_ready, 1)
            pe.wait_ge(band_step, 2 * K)

            def product(n, slot, static, g):
                buf = (slot * G + g) % GBUF
                if static != 0 or g >= GBUF:
                    pe.wait_ge(left_done, n * G + g - GBUF + 1)
                for d in range(T):
                    for c in range(T):
                        last = nc.tensor.matmul(att[:, buf, d, :], prob[:, c, d * P:(d + 1) * P],
                                                img[:, slot, c, g * GC:(g + 1) * GC],
                                                start=(c == 0), stop=(c == T - 1))
                last.then_inc(att_ready, 1)

            def left_conv(n):
                pe.wait_ge(left_rep_ready, (n + 1) * T)
                for c in range(T):
                    nc.tensor.matmul(z_left[:, 0:CH], left_rep[:, c, :], band_q[:, c, :],
                                     start=(c == 0), stop=(c == T - 1))
                for d in range(T):
                    for c in range(T):
                        last = nc.tensor.matmul(z_left[:, CH + d:CH + d + 1], band_q[:, c, d * P:(d + 1) * P],
                                                left_rep[:, c, 0:1], start=(c == 0), stop=(c == T - 1))
                last.then_inc(z_left_ready, 1)

            def total(n):
                pe.wait_ge(exp_qq_ready, (n + 1) * T)
                for c in range(T):
                    last = nc.tensor.matmul(z_left[:, TOTAL:TOTAL + 1], ones[:, :], row_sum[:, c:c + 1],
                                            start=(c == 0), stop=(c == T - 1))
                last.then_inc(total_ready, 1)

            def right_conv(n):
                pe.wait_ge(right_tot_ready, n + 1)
                for d in range(T):
                    for c in range(T):
                        last = nc.tensor.matmul(z_right[:, d:d + 1], band_loc[:, c, d * P:(d + 1) * P],
                                                right_tot[:, c:c + 1], start=(c == 0), stop=(c == T - 1))
                last.then_inc(z_right_ready, 1)

            left_conv(0)
            total(0)

            def step(n, use, slot, static):
                pe.wait_ge(prob_ready, n + 1)
                for g in range(G):
                    if g == RIGHT_CONV_AFTER + 1:
                        right_conv(n)
                    if g == LEFT_CONV_AFTER + 1 and static != N - 1:
                        left_conv(n + 1)
                    if g == TOTAL_AFTER + 1 and static != N - 1:
                        total(n + 1)
                    product(n, slot, static, g)

            images(pe, step)


_INS = ['x', 'L0_conv_w_q', 'L0_conv_b_q', 'L0_conv_w_loc', 'L0_conv_b_loc']


def kernel(**inputs):
    import numpy as _np
    import concourse.bacc as _bacc
    from concourse import mybir as _mybir
    from concourse.bass_utils import run_bass_kernel_spmd as _run

    nc = _bacc.Bacc("TRN2", target_bir_lowering=False, num_devices=1)
    arrays, args = {}, []
    for name in _INS:
        a = _np.ascontiguousarray(inputs[name])
        arrays[f"in_{name}_dram"] = a
        args.append(nc.dram_tensor(f"in_{name}_dram", a.shape, _mybir.dt.from_np(a.dtype), kind="ExternalInput").ap())
    args.append(nc.dram_tensor("out_0_dram", inputs['x'].shape, _mybir.dt.float32, kind="ExternalOutput").ap())
    gated_channel_kernel(nc, *args)
    r = _run(nc, [arrays], core_ids=[0])
    return r.results[0]["out_0_dram"]
```
